# Optimizing a Trainium2 kernel written in Bass

```python
import numpy as np
import jax
import jax.numpy as jnp

def _softmax(x, axis=-1):
    return jax.nn.softmax(x, axis=axis)

def _gelu(x):
    return jax.nn.gelu(x, approximate=True)

def _silu(x):
    return jax.nn.silu(x)

def _sigmoid(x):
    return jax.nn.sigmoid(x)

def _layernorm(x, axis=-1, eps=1e-05):
    m = jnp.mean(x, axis=axis, keepdims=True)
    v = jnp.var(x, axis=axis, keepdims=True)
    return (x - m) / jnp.sqrt(v + eps)

def _scatter_add(tgt, idx, src, axis=0):
    return tgt.at[idx].add(src)

def _segment_sum(src, seg, n):
    return jax.ops.segment_sum(src, seg, n)
kernel_name = 'mk_adj_seq_d2_adj_r2_7f30c1'

def setup_inputs(seed: int=0):
    np.random.seed(seed)
    _w = jnp.asarray

    def _rec_inputs():
        import jax
        import jax.numpy as jnp
        _gk = jax.random.key(seed)
        x = 7.22e-05 + 1 * jax.random.normal(jax.random.fold_in(_gk, 1), (32, 256, 256), jnp.float32)
        _w = (1.0 + jnp.arange(256, dtype=jnp.float32)) ** (-0.5)
        _w = _w / _w.mean()
        _pij = jnp.clip(0.015625 * _w[:, None] * _w[None, :], 0.0, 1.0)
        _a = jax.random.uniform(jax.random.fold_in(_gk, 2), (32, 256, 256)) < _pij
        adj = _a.astype(jnp.int32)
        return (x, adj)
    x, adj = _rec_inputs()

    def _L0_gnn_setup():
        import jax, jax.numpy as jnp
        import numpy as np
        import math
        D = 256
        B, L = (8, 1024)
        EPS = 1e-05

        def layer_norm(y, gamma, beta):
            mu = jnp.mean(y, axis=-1, keepdims=True)
            var = jnp.mean(jnp.square(y - mu), axis=-1, keepdims=True)
            return (y - mu) * jax.lax.rsqrt(var + EPS) * gamma + beta
        key = jax.random.key(seed)
        ks = jax.random.split(key, 8)
        s = 1.0 / math.sqrt(D)
        x = jax.random.normal(ks[0], (B, L, D), dtype=jnp.float32)
        adj = jax.random.randint(ks[1], (B, L, L), 0, 2, dtype=jnp.int32)
        Wq = jax.random.normal(ks[2], (D, D), dtype=jnp.float32) * s
        Wk = jax.random.normal(ks[3], (D, D), dtype=jnp.float32) * s
        Wv = jax.random.normal(ks[4], (D, D), dtype=jnp.float32) * s
        Wo = jax.random.normal(ks[5], (D, D), dtype=jnp.float32) * s
        bo = jnp.zeros((D,), dtype=jnp.float32)
        gamma = jnp.ones((D,), dtype=jnp.float32)
        beta = jnp.zeros((D,), dtype=jnp.float32)
        return {'x': x, 'adj': adj, 'Wq': Wq, 'Wk': Wk, 'Wv': Wv, 'Wo': Wo, 'bo': bo, 'gamma': gamma, 'beta': beta}
    _L0_gnn_all = _L0_gnn_setup()
    _L0_gnn_in = {k: v for k, v in _L0_gnn_all.items() if k in ('Wq', 'Wk', 'Wv', 'Wo', 'bo', 'gamma', 'beta')}
    del _L0_gnn_all

    def _L1_gnn_setup():
        import jax, jax.numpy as jnp
        import numpy as np
        EPSILON = 1e-13
        LN_EPS = 1e-05
        DIRECTIONS = 2
        HID = 256

        def _layer_norm(x, gamma, beta):
            mu = jnp.mean(x, axis=-1, keepdims=True)
            var = jnp.mean(jnp.square(x - mu), axis=-1, keepdims=True)
            return (x - mu) * jax.lax.rsqrt(var + LN_EPS) * gamma + beta
        key = jax.random.key(seed)
        k1, k2, k3, k4 = jax.random.split(key, 4)
        B, N, D = (16, 512, HID)
        adj = jax.random.randint(k1, (B, N, N), 0, 3, dtype=jnp.int32)
        hid = jax.random.normal(k2, (B, N, D), dtype=jnp.float32)
        W = jax.random.normal(k3, (DIRECTIONS * D, D), dtype=jnp.float32) * (1.0 / np.sqrt(DIRECTIONS * D))
        b = jnp.zeros((D,), dtype=jnp.float32)
        gamma = jnp.ones((D,), dtype=jnp.float32)
        beta = jnp.zeros((D,), dtype=jnp.float32)
        return {'adj': adj, 'hid': hid, 'W': W, 'b': b, 'gamma': gamma, 'beta': beta}
    _L1_gnn_all = _L1_gnn_setup()
    _L1_gnn_in = {k: v for k, v in _L1_gnn_all.items() if k in ('W', 'b', 'gamma', 'beta')}
    del _L1_gnn_all
    return {'x': x, 'adj': adj, 'L0_gnn_Wq': _L0_gnn_in['Wq'], 'L0_gnn_Wk': _L0_gnn_in['Wk'], 'L0_gnn_Wv': _L0_gnn_in['Wv'], 'L0_gnn_Wo': _L0_gnn_in['Wo'], 'L0_gnn_bo': _L0_gnn_in['bo'], 'L0_gnn_gamma': _L0_gnn_in['gamma'], 'L0_gnn_beta': _L0_gnn_in['beta'], 'L1_gnn_W': _L1_gnn_in['W'], 'L1_gnn_b': _L1_gnn_in['b'], 'L1_gnn_gamma': _L1_gnn_in['gamma'], 'L1_gnn_beta': _L1_gnn_in['beta']}

def reference(x, adj, L0_gnn_Wq, L0_gnn_Wk, L0_gnn_Wv, L0_gnn_Wo, L0_gnn_bo, L0_gnn_gamma, L0_gnn_beta, L1_gnn_W, L1_gnn_b, L1_gnn_gamma, L1_gnn_beta):
    import jax
    import jax.numpy as jnp

    def _L0_gnn_ref(x, adj, Wq, Wk, Wv, Wo, bo, gamma, beta):
        import jax, jax.numpy as jnp
        import numpy as np
        import math
        D = 256
        B, L = (8, 1024)
        EPS = 1e-05

        def layer_norm(y, gamma, beta):
            mu = jnp.mean(y, axis=-1, keepdims=True)
            var = jnp.mean(jnp.square(y - mu), axis=-1, keepdims=True)
            return (y - mu) * jax.lax.rsqrt(var + EPS) * gamma + beta
        d_out = Wq.shape[1]
        scale = 1.0 / math.sqrt(d_out)
        Q = x @ Wq
        K = x @ Wk
        V = x @ Wv
        sc = jnp.einsum('bld,bmd->blm', Q, K) * scale
        mask = adj == 0
        sc = jnp.where(mask, -jnp.inf, sc)
        all_inf = jnp.all(mask, axis=-1, keepdims=True)
        sc = jnp.where(all_inf, 0.0, sc)
        w = jax.nn.softmax(sc, axis=-1)
        out = jnp.einsum('blm,bmd->bld', w, V)
        y = x + out @ Wo + bo
        return layer_norm(y, gamma, beta)

    def _L1_gnn_ref(adj, hid, W, b, gamma, beta):
        import jax, jax.numpy as jnp
        import numpy as np
        EPSILON = 1e-13
        LN_EPS = 1e-05
        DIRECTIONS = 2
        HID = 256

        def _layer_norm(x, gamma, beta):
            mu = jnp.mean(x, axis=-1, keepdims=True)
            var = jnp.mean(jnp.square(x - mu), axis=-1, keepdims=True)
            return (x - mu) * jax.lax.rsqrt(var + LN_EPS) * gamma + beta
        residual = hid
        direct_list = []
        for j in range(DIRECTIONS):
            mask = (adj == j + 1).astype(hid.dtype)
            weight = mask / (jnp.sum(mask, axis=-1, keepdims=True) + EPSILON)
            direct_list.append(jnp.einsum('bnm,bmd->bnd', weight, hid))
        out = jnp.concatenate(direct_list, axis=-1)
        out = out @ W + b
        out = jax.nn.relu(out)
        out = out + residual
        return _layer_norm(out, gamma, beta)
    x = _L0_gnn_ref(x, adj, L0_gnn_Wq, L0_gnn_Wk, L0_gnn_Wv, L0_gnn_Wo, L0_gnn_bo, L0_gnn_gamma, L0_gnn_beta)
    x = _L1_gnn_ref(adj, x, L1_gnn_W, L1_gnn_b, L1_gnn_gamma, L1_gnn_beta)
    return x

_drawn_inputs = setup_inputs


def setup_inputs(seed=0):
    import zlib

    import numpy as np

    out = dict(_drawn_inputs(seed))
    spreads = {'L0_gnn_bo': (0.0, 0.1),
     'L0_gnn_gamma': (1.0, 0.2),
     'L0_gnn_beta': (0.0, 0.1),
     'L1_gnn_b': (0.0, 0.1),
     'L1_gnn_gamma': (1.0, 0.2),
     'L1_gnn_beta': (0.0, 0.1)}
    factors = {}
    for name, (base, spread) in spreads.items():
        noise = np.random.default_rng([zlib.crc32(name.encode()), seed]).standard_normal(out[name].shape)
        drawn = base * np.exp(spread * noise) if base else spread * noise
        out[name] = jnp.asarray(drawn.astype(out[name].dtype))
    for name, factor in factors.items():
        out[name] = (out[name] * factor).astype(out[name].dtype)
    return out
```

```python
from contextlib import ExitStack

import concourse.bass as bass
from concourse import mybir

F32 = mybir.dt.float32
F32R = mybir.dt.float32r
BF16 = mybir.dt.bfloat16
I32 = mybir.dt.int32
ALU = mybir.AluOpType
ACT = mybir.ActivationFunctionType

P = 128
MASKED = -(2.0 ** 100)
LN_EPS = 1e-5
DEGREE_EPS = 1e-13


def gnn_kernel(nc: bass.Bass, x, adj, Wq, Wk, Wv, Wo, bo, gamma0, beta0, W1, b1, gamma1, beta1, out):
    G, N, D = x.shape
    T = N // P
    C = D // P
    J = 2
    SCALE = float(D) ** -0.5
    ROOT = float(D) ** -0.5
    assert T == 2 and C == 2 and N == D == 256 and W1.shape[0] == J * D

    FIRST, LAST = -1, G + 2
    LOOP_FIRST = 5
    LOOP_PAIRS = (G - 3 - LOOP_FIRST) // 2
    LOOP_END = LOOP_FIRST + 2 * LOOP_PAIRS

    with ExitStack() as ctx:
        def sb(name, shape, dt=F32):
            return ctx.enter_context(nc.sbuf_tensor(name, shape, dt))

        def sem(name):
            return ctx.enter_context(nc.semaphore(name))

        def split_pair(name, shape):
            return sb(name + "_hi", shape, F32R), sb(name + "_lo", shape, F32R)

        ident = sb("ident", [P, P])
        ident_b = sb("ident_b", [P, P], BF16)
        ones_b = sb("ones_b", [P, 1], BF16)
        minus_half, eps_c = (sb(n, [P, 2 * T]) for n in ("minus_half", "eps_c"))
        wq_s, wk_s, wv_s, wo_s = (sb(n, [P, C, D]) for n in ("wq_s", "wk_s", "wv_s", "wo_s"))
        wqT, wkT, wvT = (sb(n, [P, C, D]) for n in ("wqT", "wkT", "wvT"))
        w1_s = sb("w1_s", [P, J * C, D])
        wqk_hi, wqk_lo = split_pair("wqk", [P, C, D])
        wvo_hi, wvo_lo = split_pair("wvo", [P, C, D])
        w1_hi, w1_lo = split_pair("w1", [P, J * C, D])
        bo_r, gamma0_r, beta0_r, gamma1_r, beta1_r = (
            sb(n, [P, T, D]) for n in ("bo_r", "gamma0_r", "beta0_r", "gamma1_r", "beta1_r"))
        b1_r = sb("b1_r", [P, D])

        x_s = sb("x_s", [P, 2, T, D])
        adj_s = sb("adj_s", [P, 2, T, N], I32)
        kind = sb("kind", [P, T, N], BF16)
        no_edge = sb("no_edge", [P, 2, T, N], BF16)
        maskT = sb("maskT", [P, 2, T, J, N], F32R)
        x_bo = sb("x_bo", [P, 2, T, D])
        xT_hi, xT_lo = split_pair("xT", [P, C, N])
        qT_hi, qT_lo = split_pair("qT", [P, C, N])
        v_hi, v_lo = split_pair("v", [P, T, D])
        neg_score = sb("neg_score", [P, T, N])
        neg_max = sb("neg_max", [P, T])
        prob = sb("prob", [P, T, N])
        prob_sum = sb("prob_sum", [P, 2, T])
        inv_sum = sb("inv_sum", [P, T])
        pT_hi, pT_lo = split_pair("pT", [P, T, N])
        y0 = sb("y0", [P, T, D])
        h = sb("h", [P, 2, T, D])
        h_hi, h_lo = split_pair("h", [P, T, D])
        nb_hi, nb_lo = split_pair("nb", [P, C, J * N])
        degree = sb("degree", [P, T * J])
        inv_degree = sb("inv_degree", [P, 2, T * J])
        z_a = sb("z_a", [P, T, D])
        z_b = sb("z_b", [P, T, D])
        y1 = sb("y1", [P, 2, T, D])
        square = sb("square", [P, 2 * T, D])
        ln_sum = sb("ln_sum", [P, 2, 2 * T])
        neg_mean = sb("neg_mean", [P, 2, 2 * T])
        scaled_mean = sb("scaled_mean", [P, 2, 2 * T])
        var = sb("var", [P, 2, 2 * T])
        var_eps = sb("var_eps", [P, 2 * T])
        rstd = sb("rstd", [P, 2, 2 * T])
        shift = sb("shift", [P, 2, 2 * T])

        bank = [ctx.enter_context(nc.psum_tensor(f"bank{i}", [P, 512], F32)) for i in range(8)]
        BQ, BV, BS, BZ0, BZ1, BN0, BN1, BO0 = bank
        q_ps = pT_ps = BQ
        v_ps = xT_ps = BV
        s_ps = BS
        kindT_ps = BS[:, :].bitcast(BF16)[:, 0:T * N]
        z_ps = [BZ0, BZ1]
        o_ps = [BO0, BZ0]
        nb_ps = [BN0, BN1]
        deg_ps = BZ1[:, 0:T * J]

        qk_in, vo_in, w1_in, vectors_in = (sem(n) for n in ("qk_in", "vo_in", "w1_in", "vectors_in"))
        x_in = [sem("x_in0"), sem("x_in1")]
        adj_in = [sem("adj_in0"), sem("adj_in1")]
        stored = [sem("stored0"), sem("stored1")]
        zeros_set, ident_set, const_set = sem("zeros_set"), sem("ident_set"), sem("const_set")
        wT_made, wT_out, w_made, w_hi_set, w_ready = (
            sem(n) for n in ("wT_made", "wT_out", "w_made", "w_hi_set", "w_ready"))
        xT_made, kindT_made, q_made, v_made, s_made, z_made, pT_made, o_made, nb_made, deg_made = (
            sem(n) for n in ("xT_made", "kindT_made", "q_made", "v_made", "s_made", "z_made",
                             "pT_made", "o_made", "nb_made", "deg_made"))
        q_hi_set, v_hi_set, xT_hi_set, pT_hi_set, nb_hi_set, h_hi_set = (
            sem(n) for n in ("q_hi_set", "v_hi_set", "xT_hi_set", "pT_hi_set", "nb_hi_set", "h_hi_set"))
        prob_set, squares_set, norm0_set, norm1_set = (
            sem(n) for n in ("prob_set", "squares_set", "norm0_set", "norm1_set"))
        kind_set, no_edge_set, masks_set, q_lo_set, v_lo_set, xT_lo_set, pT_lo_set, nb_lo_set = (
            sem(n) for n in ("kind_set", "no_edge_set", "masks_set", "q_lo_set", "v_lo_set",
                             "xT_lo_set", "pT_lo_set", "nb_lo_set"))
        scored, inv_sum_set, degree_set, inv_degree_set, z_a_set, z_b_set, y0_set, y1_set = (
            sem(n) for n in ("scored", "inv_sum_set", "degree_set", "inv_degree_set", "z_a_set",
                             "z_b_set", "y0_set", "y1_set"))
        x_bo_set, mean_set, neg_mean_set, var_set, rstd_set, shift_set, scaled0, h_set, h_lo_set, scaled1, out_set = (
            sem(n) for n in ("x_bo_set", "mean_set", "neg_mean_set", "var_set", "rstd_set", "shift_set", "scaled0",
                             "h_set", "h_lo_set", "scaled1", "out_set"))

        def there(c):
            return 0 <= c < G

        def columns(c):
            return slice(0 if there(c - 2) else T, 2 * T if there(c) else T)

        def wait(eng, s, value):
            if not isinstance(value, int) or value > 0:
                eng.wait_ge(s, value)

        def steps(eng, step):
            for c in range(FIRST, LOOP_FIRST):
                step(0, c)
            with eng.Fori(0, LOOP_PAIRS) as pair:
                for b in range(2):
                    step(2 * pair, LOOP_FIRST + b)
            for c in range(LOOP_END, LAST + 1):
                step(0, c)

        def dma_count(p, c):
            return 8 * p + 16 * (c // 2 + 1)

        VECTORS_IN = 16 * (5 * T + 1)

        block = ctx.enter_context(nc.Block())

        @block.sync
        def _(sp):
            def load(p, c):
                sp.dma_start(x_s[:, c % 2, :, :], x[p + c].rearrange("(t p) d -> p t d", p=P))\
                  .then_inc(x_in[c % 2], 16)

            def load_adj(p, c):
                sp.dma_start(adj_s[:, c % 2, :, :], adj[p + c].rearrange("(t p) m -> p t m", p=P))\
                  .then_inc(adj_in[c % 2], 16)

            for w, s in ((Wq, wq_s), (Wk, wk_s)):
                sp.dma_start(s[:, :, :], w.rearrange("(c p) e -> p c e", p=P)).then_inc(qk_in, 16)
            load(0, 0)
            load_adj(0, 0)
            load(0, 1)
            load_adj(0, 1)

            def step(p, c):
                if there(c + 3):
                    wait(sp, xT_made, p + c + 2)
                    wait(sp, x_bo_set, p + c + 2)
                    load(p, c + 3)
                    wait(sp, kind_set, p + c + 2)
                    load_adj(p, c + 3)
                if there(c - 3):
                    wait(sp, out_set, p + c - 2)
                    sp.dma_start(out[p + c - 3].rearrange("(t p) d -> p t d", p=P),
                                 y1[:, (c - 3) % 2, :, :]).then_inc(stored[(c - 3) % 2], 16)

            steps(sp, step)
            for s in stored:
                sp.wait_ge(s, 16 * (G // 2))

        @block.tensor
        def _(pe):
            def product(dst, lhs, rhs, first, last):
                (a_hi, a_lo), (b_hi, b_lo) = lhs, rhs
                pe.matmul(dst, a_lo, b_hi, start=first, stop=False)
                pe.matmul(dst, a_hi, b_lo, start=False, stop=False)
                return pe.matmul(dst, a_hi, b_hi, start=False, stop=last)

            pe.wait_ge(ident_set, 1)
            for n, (w, ps) in enumerate(((wq_s, BQ), (wk_s, BV), (wv_s, BS))):
                pe.wait_ge(qk_in if n < 2 else vo_in, 32)
                for k in range(C):
                    for e in range(C):
                        mm = pe.transpose(ps[:, e * D + k * P:e * D + (k + 1) * P],
                                          w[:, k, e * P:(e + 1) * P], ident[:, :])
                mm.then_inc(wT_made, 1)
            for n, (lhs, rhs, ps) in enumerate(((wqT, wkT, BZ0), (wvT, wo_s, BZ1))):
                pe.wait_ge(wT_out, 2 + n)
                for k in range(C):
                    for e in range(C):
                        mm = pe.matmul(ps[:, k * D:(k + 1) * D], lhs[:, e, k * P:(k + 1) * P],
                                       rhs[:, e, :], start=(e == 0), stop=(e == C - 1))
                mm.then_inc(w_made, 1)

            def z_tile(p, c, t):
                for j in range(J):
                    for d in range(C):
                        cols = slice(j * N + t * P, j * N + (t + 1) * P)
                        mm = product(z_ps[t][:, j * D:(j + 1) * D],
                                     (nb_hi[:, d, cols], nb_lo[:, d, cols]),
                                     (w1_hi[:, j * C + d, :], w1_lo[:, j * C + d, :]),
                                     d == 0, d == C - 1)
                mm.then_inc(z_made, 1)

            def step(p, c):
                if there(c):
                    if c == 0:
                        pe.wait_ge(w_ready, 3)
                    wait(pe, xT_lo_set, p + c + 1)
                    for d in range(C):
                        for k in range(C):
                            cols = slice(d * P, (d + 1) * P)
                            mm = product(q_ps[:, d * N:(d + 1) * N],
                                         (wqk_hi[:, k, cols], wqk_lo[:, k, cols]),
                                         (xT_hi[:, k, :], xT_lo[:, k, :]), k == 0, k == C - 1)
                    mm.then_inc(q_made, 1)
                    for t in range(T):
                        for k in range(C):
                            rows = slice(t * P, (t + 1) * P)
                            mm = product(v_ps[:, t * D:(t + 1) * D],
                                         (xT_hi[:, k, rows], xT_lo[:, k, rows]),
                                         (wvo_hi[:, k, :], wvo_lo[:, k, :]), k == 0, k == C - 1)
                    mm.then_inc(v_made, 1)
                    wait(pe, q_lo_set, p + c + 1)
                    wait(pe, masks_set, p + c + 1)
                    for t in range(T):
                        for d in range(C):
                            rows = slice(t * P, (t + 1) * P)
                            mm = product(s_ps[:, t * N:(t + 1) * N],
                                         (qT_hi[:, d, rows], qT_lo[:, d, rows]),
                                         (xT_hi[:, d, :], xT_lo[:, d, :]), d == 0, d == C - 1)
                    mm.then_inc(s_made, 1)
                if there(c - 2):
                    wait(pe, nb_lo_set, C * (p + c - 1))
                    wait(pe, y0_set, T * min(c, G) if isinstance(p, int) else T * (p + c))
                    z_tile(p, c, 0)
                if there(c + 1):
                    wait(pe, x_in[(c + 1) % 2], dma_count(p, c + 1))
                    wait(pe, v_lo_set, p + c + 1)
                    if c == -1:
                        pe.wait_ge(wT_out, 3)
                    for t in range(T):
                        for k in range(C):
                            mm = pe.transpose(xT_ps[:, k * N + t * P:k * N + (t + 1) * P],
                                              x_s[:, (c + 1) % 2, t, k * P:(k + 1) * P], ident[:, :])
                    mm.then_inc(xT_made, 1)
                    wait(pe, kind_set, p + c + 2)
                    wait(pe, scored, T * (p + c + 1))
                    if c == -1:
                        pe.wait_ge(ident_set, 2)
                    for t in range(T):
                        for m in range(T):
                            mm = pe.transpose(kindT_ps[:, m * N + t * P:m * N + (t + 1) * P],
                                              kind[:, t, m * P:(m + 1) * P], ident_b[:, :])
                    mm.then_inc(kindT_made, 1)
                if there(c):
                    wait(pe, prob_set, T * (p + c + 1))
                    for t in range(T):
                        for m in range(T):
                            mm = pe.transpose(pT_ps[:, m * N + t * P:m * N + (t + 1) * P],
                                              prob[:, t, m * P:(m + 1) * P], ident[:, :])
                    mm.then_inc(pT_made, 1)
                if there(c - 2):
                    wait(pe, degree_set, p + c - 1)
                    z_tile(p, c, 1)
                if there(c):
                    wait(pe, pT_lo_set, p + c + 1)
                    wait(pe, v_lo_set, p + c + 1)
                    wait(pe, y0_set, T * (p + c))
                    for t in range(T):
                        if t == 1:
                            wait(pe, z_b_set, T * (p + c - 2) + 1)
                        for m in range(T):
                            rows = slice(t * P, (t + 1) * P)
                            mm = product(o_ps[t][:, 0:D], (pT_hi[:, m, rows], pT_lo[:, m, rows]),
                                         (v_hi[:, m, :], v_lo[:, m, :]), m == 0, m == T - 1)
                        mm.then_inc(o_made, 1)
                if there(c - 1):
                    g = (c - 1) % 2
                    wait(pe, h_hi_set, p + c)
                    wait(pe, h_lo_set, p + c)
                    for d in range(C):
                        wait(pe, nb_lo_set, C * (p + c - 2) + d + 1)
                        for n, part in enumerate((h_lo, h_hi)):
                            for m in range(T):
                                mm = pe.matmul(nb_ps[d][:, :], part[:, m, d * P:(d + 1) * P],
                                               maskT[:, g, m, :, :].rearrange("p j n -> p (j n)"),
                                               start=(n == 0 and m == 0), stop=(n == 1 and m == T - 1))
                        mm.then_inc(nb_made, 1)
                    wait(pe, z_b_set, T * (p + c - 1))
                    for t in range(T):
                        for j in range(J):
                            for m in range(T):
                                mask_b = maskT[:, g, m, j, :].bitcast(BF16)[:, 2 * t * P + 1:2 * (t + 1) * P:2]
                                mm = pe.matmul(deg_ps[:, t * J + j:t * J + j + 1], mask_b, ones_b[:, :],
                                               start=(m == 0), stop=(m == T - 1))
                    mm.then_inc(deg_made, 1)

            steps(pe, step)

        @block.scalar
        def _(act):
            for w, s in ((Wv, wv_s), (Wo, wo_s)):
                act.dma_start(s[:, :, :], w.rearrange("(c p) e -> p c e", p=P)).then_inc(vo_in, 16)
            act.dma_start(w1_s[:, :, :], W1.rearrange("(c p) e -> p c e", p=P)).then_inc(w1_in, 16)
            for v, s in ((bo, bo_r), (gamma0, gamma0_r), (beta0, beta0_r), (gamma1, gamma1_r), (beta1, beta1_r)):
                for t in range(T):
                    act.dma_start(s[:, t, :], v.partition_broadcast(P)).then_inc(vectors_in, 16)
            act.dma_start(b1_r[:, :], b1.partition_broadcast(P)).then_inc(vectors_in, 16)

            act.wait_ge(w1_in, 16)
            act.activation(w1_hi[:, :, :], w1_s[:, :, :], ACT.Copy).then_inc(w_hi_set, 1)
            for n, (hi, ps) in enumerate(((wqk_hi, BZ0), (wvo_hi, BZ1))):
                act.wait_ge(w_made, n + 1)
                act.activation(hi[:, :, :].rearrange("p c n -> p (c n)"), ps[:, :], ACT.Copy)\
                   .then_inc(w_hi_set, 1)

            def flat(a):
                return a[:, :, :].rearrange("p c n -> p (c n)")

            def norm(col, y, p, c):
                g = (c - 1) % 2
                return act.activation(y, y, ACT.Identity, bias=shift[:, g, col:col + 1],
                                      scale=rstd[:, g, col:col + 1])

            def squares(col, y, p, c):
                g = c % 2
                act.activation(square[:, col, :], y, ACT.Square, bias=scaled_mean[:, g, col:col + 1],
                               scale=ROOT, accum_out=var[:, g, col:col + 1]).then_inc(squares_set, 1)

            def step(p, c):
                if there(c):
                    wait(act, q_made, p + c + 1)
                    act.activation(flat(qT_hi), q_ps[:, :], ACT.Copy).then_inc(q_hi_set, 1)
                if there(c - 1):
                    wait(act, shift_set, p + c)
                    for t in range(T):
                        norm(T + t, y0[:, t, :], p, c).then_inc(norm0_set, 1)
                if there(c):
                    wait(act, v_made, p + c + 1)
                    act.activation(flat(v_hi), v_ps[:, :], ACT.Copy).then_inc(v_hi_set, 1)
                    for t in range(T):
                        wait(act, scored, T * (p + c) + t + 1)
                        act.activation(prob[:, t, :], neg_score[:, t, :], ACT.Exp, scale=-1.0,
                                       bias=neg_max[:, t:t + 1],
                                       accum_out=prob_sum[:, c % 2, t:t + 1]).then_inc(prob_set, 1)
                if there(c + 1):
                    wait(act, xT_made, p + c + 2)
                    act.activation(flat(xT_hi), xT_ps[:, :], ACT.Copy).then_inc(xT_hi_set, 1)
                if there(c):
                    wait(act, pT_made, p + c + 1)
                    act.activation(flat(pT_hi), pT_ps[:, :], ACT.Copy).then_inc(pT_hi_set, 1)
                if there(c - 1):
                    wait(act, h_set, p + c)
                    wait(act, nb_made, C * (p + c - 1))
                    act.activation(flat(h_hi), h[:, (c - 1) % 2, :, :].rearrange("p t d -> p (t d)"),
                                   ACT.Copy).then_inc(h_hi_set, 1)
                if there(c - 3):
                    wait(act, shift_set, p + c)
                    for t in range(T):
                        norm(t, y1[:, (c - 3) % 2, t, :], p, c).then_inc(norm1_set, 1)
                if there(c - 1):
                    wait(act, nb_made, C * (p + c - 1) + 1)
                    act.activation(nb_hi[:, 0, :], nb_ps[0][:, :], ACT.Copy).then_inc(nb_hi_set, 1)
                if there(c - 2):
                    wait(act, mean_set, p + c + 1)
                    for t in range(T):
                        squares(t, y1[:, (c - 2) % 2, t, :], p, c)
                if there(c - 1):
                    wait(act, nb_made, C * (p + c))
                    act.activation(nb_hi[:, 1, :], nb_ps[1][:, :], ACT.Copy).then_inc(nb_hi_set, 1)
                if there(c):
                    wait(act, mean_set, p + c + 1)
                    for t in range(T):
                        squares(T + t, y0[:, t, :], p, c)

            steps(act, step)

        @block.vector
        def _(dve):
            def flat(a):
                return a[:, :, :].rearrange("p c n -> p (c n)")

            def low(lo, full, hi):
                return dve.tensor_tensor(lo, full, hi.bitcast(F32), ALU.subtract)

            for n, (wT, ps) in enumerate(((wqT, BQ), (wkT, BV), (wvT, BS))):
                dve.wait_ge(wT_made, n + 1)
                dve.tensor_copy(flat(wT), ps[:, :]).then_inc(wT_out, 1)
            dve.wait_ge(w_hi_set, 1)
            low(flat(w1_lo), flat(w1_s), flat(w1_hi)).then_inc(w_ready, 1)
            for n, (lo, hi, ps) in enumerate(((wqk_lo, wqk_hi, BZ0), (wvo_lo, wvo_hi, BZ1))):
                dve.wait_ge(w_hi_set, n + 2)
                low(flat(lo), ps[:, :], flat(hi)).then_inc(w_ready, 1)
            dve.wait_ge(vectors_in, VECTORS_IN)

            def masks(p, c):
                wait(dve, kindT_made, p + c + 1)
                wait(dve, nb_made, C * (p + c - 1))
                wait(dve, deg_made, p + c - 1)
                for j in range(J):
                    ins = dve.tensor_scalar(maskT[:, c % 2, :, j, :],
                                            kindT_ps.rearrange("p (m n) -> p m n", m=T),
                                            float(j + 1), None, ALU.is_equal)
                ins.then_inc(masks_set, 1)

            def edge_kind(p, c):
                wait(dve, adj_in[c % 2], dma_count(p, c))
                wait(dve, kindT_made, p + c)
                dve.tensor_scalar(kind[:, :, :], adj_s[:, c % 2, :, :], -1.0, 3.0, ALU.max, ALU.min)\
                   .then_inc(kind_set, 1)

            def edge_mask(p, c):
                wait(dve, kind_set, p + c + 1)
                dve.tensor_scalar(no_edge[:, c % 2, :, :], kind[:, :, :], 0.0, MASKED,
                                  ALU.is_equal, ALU.mult).then_inc(no_edge_set, 1)

            def z_first(p, c, t):
                wait(dve, z_made, T * (p + c) + t + 1)
                wait(dve, inv_degree_set, p + c + 1)
                dve.scalar_tensor_tensor(out=z_a[:, t, :], in0=z_ps[t][:, 0:D],
                                         scalar=inv_degree[:, c % 2, t * J:t * J + 1], in1=b1_r[:, :],
                                         op0=ALU.mult, op1=ALU.add).then_inc(z_a_set, 1)

            def z_second(p, c, t):
                wait(dve, z_a_set, T * (p + c) + t + 1)
                dve.scalar_tensor_tensor(out=z_b[:, t, :], in0=z_ps[t][:, D:2 * D],
                                         scalar=inv_degree[:, c % 2, t * J + 1:t * J + 2],
                                         in1=z_a[:, t, :], op0=ALU.mult, op1=ALU.add).then_inc(z_b_set, 1)

            def relu_residual(p, c, t):
                wait(dve, z_b_set, T * (p + c) + t + 1)
                wait(dve, stored[c % 2], dma_count(p, c - 2))
                dve.scalar_tensor_tensor(out=y1[:, c % 2, t, :], in0=z_b[:, t, :], scalar=0.0,
                                         in1=h[:, c % 2, t, :], op0=ALU.max, op1=ALU.add,
                                         accum_out=ln_sum[:, c % 2, t:t + 1]).then_inc(y1_set, 1)

            def attention_residual(p, c, t):
                wait(dve, o_made, T * (p + c) + t + 1)
                wait(dve, inv_sum_set, p + c + 1)
                wait(dve, x_bo_set, p + c + 1)
                wait(dve, h_set, p + c)
                dve.scalar_tensor_tensor(out=y0[:, t, :], in0=o_ps[t][:, 0:D], scalar=inv_sum[:, t:t + 1],
                                         in1=x_bo[:, c % 2, t, :], op0=ALU.mult, op1=ALU.add,
                                         accum_out=ln_sum[:, c % 2, T + t:T + t + 1]).then_inc(y0_set, 1)

            def step(p, c):
                if there(c):
                    masks(p, c)
                if there(c - 2):
                    wait(dve, nb_hi_set, C * (p + c - 1))
                    low(nb_lo[:, 1, :], nb_ps[1][:, :], nb_hi[:, 1, :]).then_inc(nb_lo_set, 1)
                if there(c):
                    wait(dve, q_hi_set, p + c + 1)
                    low(flat(qT_lo), q_ps[:, :], flat(qT_hi)).then_inc(q_lo_set, 1)
                if there(c - 2):
                    wait(dve, deg_made, p + c - 1)
                    dve.tensor_scalar(degree[:, :], deg_ps, DEGREE_EPS, None, ALU.add).then_inc(degree_set, 1)
                if there(c + 1):
                    edge_kind(p, c + 1)
                if there(c - 2):
                    wait(dve, degree_set, p + c - 1)
                    dve.reciprocal(inv_degree[:, c % 2, :], degree[:, :]).then_inc(inv_degree_set, 1)
                if there(c + 1):
                    edge_mask(p, c + 1)
                if there(c):
                    wait(dve, v_hi_set, p + c + 1)
                    low(flat(v_lo), v_ps[:, :], flat(v_hi)).then_inc(v_lo_set, 1)
                    dve.wait_ge(vectors_in, VECTORS_IN)
                    wait(dve, s_made, p + c + 1)
                    wait(dve, no_edge_set, p + c + 1)
                    for t in range(T):
                        dve.tensor_tensor_reduce(out=neg_score[:, t, :], in0=s_ps[:, t * N:(t + 1) * N],
                                                 in1=no_edge[:, c % 2, t, :], scale=-SCALE, scalar=3.0e38,
                                                 op0=ALU.add, op1=ALU.min,
                                                 accum_out=neg_max[:, t:t + 1]).then_inc(scored, 1)
                if there(c - 2):
                    z_first(p, c - 2, 0)
                if there(c + 1):
                    wait(dve, xT_hi_set, p + c + 2)
                    low(flat(xT_lo), xT_ps[:, :], flat(xT_hi)).then_inc(xT_lo_set, 1)
                if there(c - 2):
                    z_second(p, c - 2, 0)
                if there(c):
                    wait(dve, pT_hi_set, p + c + 1)
                    low(flat(pT_lo), pT_ps[:, :], flat(pT_hi)).then_inc(pT_lo_set, 1)
                if there(c - 2):
                    relu_residual(p, c - 2, 0)
                    z_first(p, c - 2, 1)
                if there(c):
                    wait(dve, prob_set, T * (p + c + 1))
                    dve.reciprocal(inv_sum[:, :], prob_sum[:, c % 2, :]).then_inc(inv_sum_set, 1)
                if there(c - 2):
                    z_second(p, c - 2, 1)
                if there(c):
                    attention_residual(p, c, 0)
                if there(c - 2):
                    relu_residual(p, c - 2, 1)
                if there(c):
                    attention_residual(p, c, 1)
                if there(c) or there(c - 2):
                    s = columns(c)
                    wait(dve, y1_set, T * min(c - 1, G) if isinstance(p, int) else T * (p + c - 1))
                    wait(dve, y0_set, T * min(c + 1, G) if isinstance(p, int) else T * (p + c + 1))
                    wait(dve, shift_set, p + c - 1)
                    dve.tensor_scalar(scaled_mean[:, c % 2, s], ln_sum[:, c % 2, s], -ROOT / D, None, ALU.mult)\
                       .then_inc(mean_set, 1)
                    dve.tensor_scalar(neg_mean[:, c % 2, s], ln_sum[:, c % 2, s], -1.0 / D, None, ALU.mult)\
                       .then_inc(neg_mean_set, 1)
                if there(c - 1):
                    wait(dve, nb_hi_set, C * (p + c - 1) + 1)
                    low(nb_lo[:, 0, :], nb_ps[0][:, :], nb_hi[:, 0, :]).then_inc(nb_lo_set, 1)

            steps(dve, step)

        @block.gpsimd
        def _(pool):
            for n, m in enumerate((ident, ident_b)):
                pool.memset(m[:, :], 0.0).then_inc(zeros_set, 1)
                pool.wait_ge(zeros_set, n + 1)
                pool.affine_select(out=m[:, :], in_=m[:, :], compare_op=ALU.not_equal, fill=1.0, base=0,
                                   pattern=[[-1, P]], channel_multiplier=1).then_inc(ident_set, 1)
            pool.memset(ones_b[:, :], 1.0).then_inc(const_set, 1)
            for m, value in ((minus_half, -0.5), (eps_c, LN_EPS)):
                pool.memset(m[:, :], value).then_inc(const_set, 1)
            pool.wait_ge(const_set, 3)
            pool.wait_ge(vectors_in, VECTORS_IN)

            def step(p, c):
                if there(c - 1) or there(c - 3):
                    s, g = columns(c - 1), (c - 1) % 2
                    squares = T * (max(0, min(c, G)) + max(0, min(c - 2, G))) if isinstance(p, int) \
                        else T * (2 * p + 2 * c - 2)
                    wait(pool, squares_set, squares)
                    pool.tensor_tensor(var_eps[:, s], var[:, g, s], eps_c[:, s], ALU.add)\
                        .then_inc(var_set, 1)
                    wait(pool, var_set, p + c)
                    pool.tensor_tensor(rstd[:, g, s], var_eps[:, s], minus_half[:, s], ALU.pow)\
                        .then_inc(rstd_set, 1)
                    wait(pool, rstd_set, p + c)
                    wait(pool, neg_mean_set, p + c)
                    pool.tensor_tensor(shift[:, g, s], neg_mean[:, g, s], rstd[:, g, s], ALU.mult)\
                        .then_inc(shift_set, 1)
                if there(c + 1):
                    g = (c + 1) % 2
                    wait(pool, x_in[g], dma_count(p, c + 1))
                    wait(pool, y0_set, T * (p + c))
                    pool.tensor_tensor(x_bo[:, g, :, :], x_s[:, g, :, :], bo_r[:, :, :], ALU.add)\
                        .then_inc(x_bo_set, 1)
                if there(c - 1):
                    g = (c - 1) % 2
                    wait(pool, norm0_set, T * (p + c))
                    pool.tensor_tensor(y0[:, :, :], y0[:, :, :], gamma0_r[:, :, :], ALU.mult)\
                        .then_inc(scaled0, 1)
                    wait(pool, scaled0, p + c)
                    wait(pool, y1_set, T * (p + c - 2))
                    pool.tensor_tensor(h[:, g, :, :], y0[:, :, :], beta0_r[:, :, :], ALU.add)\
                        .then_inc(h_set, 1)
                    wait(pool, h_hi_set, p + c)
                    wait(pool, nb_made, C * (p + c - 1))
                    pool.tensor_tensor(h_lo[:, :, :], h[:, g, :, :], h_hi[:, :, :].bitcast(F32),
                                       ALU.subtract).then_inc(h_lo_set, 1)
                if there(c - 3):
                    y = y1[:, (c - 3) % 2, :, :]
                    wait(pool, norm1_set, T * (p + c - 2))
                    pool.tensor_tensor(y, y, gamma1_r[:, :, :], ALU.mult).then_inc(scaled1, 1)
                    wait(pool, scaled1, p + c - 2)
                    pool.tensor_tensor(y, y, beta1_r[:, :, :], ALU.add).then_inc(out_set, 1)

            steps(pool, step)


_INS = ['x', 'adj', 'L0_gnn_Wq', 'L0_gnn_Wk', 'L0_gnn_Wv', 'L0_gnn_Wo', 'L0_gnn_bo', 'L0_gnn_gamma',
        'L0_gnn_beta', 'L1_gnn_W', 'L1_gnn_b', 'L1_gnn_gamma', 'L1_gnn_beta']


def kernel(**inputs):
    import numpy as _np
    import concourse.bacc as _bacc
    from concourse import mybir as _mybir
    from concourse.bass_utils import run_bass_kernel_spmd as _run

    nc = _bacc.Bacc("TRN2", target_bir_lowering=False, num_devices=1)
    arrays, args = {}, []
    for name in _INS:
        a = _np.ascontiguousarray(inputs[name])
        arrays[f"in_{name}_dram"] = a
        args.append(nc.dram_tensor(f"in_{name}_dram", a.shape, _mybir.dt.from_np(a.dtype),
                                   kind="ExternalInput").ap())
    args.append(nc.dram_tensor("out_dram", inputs["x"].shape, _mybir.dt.float32, kind="ExternalOutput").ap())
    gnn_kernel(nc, *args)
    r = _run(nc, [arrays], core_ids=[0])
    return r.results[0]["out_dram"]
```

```python
from contextlib import ExitStack

import concourse.bass as bass
from concourse import mybir

F32 = mybir.dt.float32
F32R = mybir.dt.float32r
BF16 = mybir.dt.bfloat16
I32 = mybir.dt.int32
ALU = mybir.AluOpType
ACT = mybir.ActivationFunctionType

P = 128
MASKED = -(2.0 ** 100)
LN_EPS = 1e-5
DEGREE_EPS = 1e-13


def gnn_kernel(nc: bass.Bass, x, adj, Wq, Wk, Wv, Wo, bo, gamma0, beta0, W1, b1, gamma1, beta1, out):
    G, N, D = x.shape
    T = N // P
    C = D // P
    J = 2
    SCALE = float(D) ** -0.5
    ROOT = float(D) ** -0.5
    assert T == 2 and C == 2 and N == D == 256 and W1.shape[0] == J * D

    FIRST, LAST = -1, G + 2
    LOOP_FIRST = 5
    LOOP_PAIRS = (G - 3 - LOOP_FIRST) // 2
    LOOP_END = LOOP_FIRST + 2 * LOOP_PAIRS

    with ExitStack() as ctx:
        def sb(name, shape, dt=F32):
            return ctx.enter_context(nc.sbuf_tensor(name, shape, dt))

        def sem(name):
            return ctx.enter_context(nc.semaphore(name))

        def split_pair(name, shape):
            return sb(name + "_hi", shape, F32R), sb(name + "_lo", shape, F32R)

        ident = sb("ident", [P, P])
        ident_b = sb("ident_b", [P, P], BF16)
        ones_b = sb("ones_b", [P, 1], BF16)
        minus_half, eps_c = (sb(n, [P, 2 * T]) for n in ("minus_half", "eps_c"))
        wq_s, wk_s, wv_s, wo_s = (sb(n, [P, C, D]) for n in ("wq_s", "wk_s", "wv_s", "wo_s"))
        wqT, wkT, wvT = (sb(n, [P, C, D]) for n in ("wqT", "wkT", "wvT"))
        w1_s = sb("w1_s", [P, J * C, D])
        wqk_hi, wqk_lo = split_pair("wqk", [P, C, D])
        wvo_hi, wvo_lo = split_pair("wvo", [P, C, D])
        w1_hi, w1_lo = split_pair("w1", [P, J * C, D])
        bo_r, gamma0_r, beta0_r, gamma1_r, beta1_r = (
            sb(n, [P, T, D]) for n in ("bo_r", "gamma0_r", "beta0_r", "gamma1_r", "beta1_r"))
        b1_r = sb("b1_r", [P, D])

        x_s = sb("x_s", [P, 2, T, D])
        adj_s = sb("adj_s", [P, 2, T, N], I32)
        kind = sb("kind", [P, T, N], BF16)
        no_edge = sb("no_edge", [P, 2, T, N], BF16)
        maskT = sb("maskT", [P, 2, T, J, N], F32R)
        x_bo = sb("x_bo", [P, 2, T, D])
        xT_hi, xT_lo = split_pair("xT", [P, C, N])
        qT_hi, qT_lo = split_pair("qT", [P, C, N])
        v_hi, v_lo = split_pair("v", [P, T, D])
        neg_score = sb("neg_score", [P, T, N])
        neg_max = sb("neg_max", [P, T])
        prob = sb("prob", [P, T, N])
        prob_sum = sb("prob_sum", [P, 2, T])
        inv_sum = sb("inv_sum", [P, T])
        pT_hi, pT_lo = split_pair("pT", [P, T, N])
        y0 = sb("y0", [P, T, D])
        h = sb("h", [P, 2, T, D])
        h_hi, h_lo = split_pair("h", [P, T, D])
        nb_hi, nb_lo = split_pair("nb", [P, C, J * N])
        degree = sb("degree", [P, T * J])
        inv_degree = sb("inv_degree", [P, 2, T * J])
        z_a = sb("z_a", [P, T, D])
        z_b = sb("z_b", [P, T, D])
        y1 = sb("y1", [P, 2, T, D])
        square = sb("square", [P, 2 * T, D])
        ln_sum = sb("ln_sum", [P, 2, 2 * T])
        neg_mean = sb("neg_mean", [P, 2, 2 * T])
        scaled_mean = sb("scaled_mean", [P, 2, 2 * T])
        var = sb("var", [P, 2, 2 * T])
        var_eps = sb("var_eps", [P, 2 * T])
        rstd = sb("rstd", [P, 2, 2 * T])
        shift = sb("shift", [P, 2, 2 * T])

        bank = [ctx.enter_context(nc.psum_tensor(f"bank{i}", [P, 512], F32)) for i in range(8)]
        BQ, BV, BS, BZ0, BZ1, BN0, BN1, BO0 = bank
        q_ps = pT_ps = BQ
        v_ps = xT_ps = BV
        s_ps = BS
        deg_ps = BS[:, 0:T * J]
        z_ps = [BZ0, BZ1]
        o_ps = [BO0, BZ0]
        kindT_ps = BO0[:, :].bitcast(BF16)[:, 0:T * N]
        nb_ps = [BN0, BN1]

        qk_in, vo_in, w1_in, vectors_in = (sem(n) for n in ("qk_in", "vo_in", "w1_in", "vectors_in"))
        x_in = [sem("x_in0"), sem("x_in1")]
        adj_in = [sem("adj_in0"), sem("adj_in1")]
        stored = [sem("stored0"), sem("stored1")]
        zeros_set, ident_set, const_set = sem("zeros_set"), sem("ident_set"), sem("const_set")
        wT_made, wT_out, w_made, w_hi_set, w_ready = (
            sem(n) for n in ("wT_made", "wT_out", "w_made", "w_hi_set", "w_ready"))
        xT_made, kindT_made, q_made, v_made, s_made, z_made, pT_made, o_made, nb_made, deg_made = (
            sem(n) for n in ("xT_made", "kindT_made", "q_made", "v_made", "s_made", "z_made",
                             "pT_made", "o_made", "nb_made", "deg_made"))
        q_hi_set, v_hi_set, xT_hi_set, pT_hi_set, nb_hi_set, h_hi_set = (
            sem(n) for n in ("q_hi_set", "v_hi_set", "xT_hi_set", "pT_hi_set", "nb_hi_set", "h_hi_set"))
        prob_set = sem("prob_set")
        squares_set = [sem("squares0_set"), sem("squares1_set")]
        norm_set = [sem("norm0_set"), sem("norm1_set")]
        kind_set, no_edge_set, masks_set, q_lo_set, v_lo_set, xT_lo_set, pT_lo_set, nb_lo_set = (
            sem(n) for n in ("kind_set", "no_edge_set", "masks_set", "q_lo_set", "v_lo_set",
                             "xT_lo_set", "pT_lo_set", "nb_lo_set"))
        mean_set = [sem("mean0_set"), sem("mean1_set")]
        neg_mean_set = [sem("neg_mean0_set"), sem("neg_mean1_set")]
        scored, inv_sum_set, degree_set, inv_degree_set, z_a_set, z_b_set, y0_set, y1_set = (
            sem(n) for n in ("scored", "inv_sum_set", "degree_set", "inv_degree_set", "z_a_set",
                             "z_b_set", "y0_set", "y1_set"))
        x_bo_set, scaled0, h_set, h_lo_set, scaled1, out_set = (
            sem(n) for n in ("x_bo_set", "scaled0", "h_set", "h_lo_set", "scaled1", "out_set"))
        var_set = [sem("var0_set"), sem("var1_set")]
        rstd_set = [sem("rstd0_set"), sem("rstd1_set")]
        shift_set = [sem("shift0_set"), sem("shift1_set")]

        def there(c):
            return 0 <= c < G

        def wait(eng, s, value):
            if not isinstance(value, int) or value > 0:
                eng.wait_ge(s, value)

        def steps(eng, step, after_first=lambda: None):
            step(0, FIRST)
            after_first()
            for c in range(FIRST + 1, LOOP_FIRST):
                step(0, c)
            with eng.Fori(0, LOOP_PAIRS) as pair:
                for b in range(2):
                    step(2 * pair, LOOP_FIRST + b)
            for c in range(LOOP_END, LAST + 1):
                step(0, c)

        def dma_count(p, c):
            return 8 * p + 16 * (c // 2 + 1)

        VECTORS_IN = 16 * (5 * T + 1)

        block = ctx.enter_context(nc.Block())

        @block.sync
        def _(sp):
            def load(p, c):
                sp.dma_start(x_s[:, c % 2, :, :], x[p + c].rearrange("(t p) d -> p t d", p=P))\
                  .then_inc(x_in[c % 2], 16)

            def load_adj(p, c):
                sp.dma_start(adj_s[:, c % 2, :, :], adj[p + c].rearrange("(t p) m -> p t m", p=P))\
                  .then_inc(adj_in[c % 2], 16)

            for w, s in ((Wq, wq_s), (Wk, wk_s)):
                sp.dma_start(s[:, :, :], w.rearrange("(c p) e -> p c e", p=P)).then_inc(qk_in, 16)
            load(0, 0)
            load_adj(0, 0)
            load(0, 1)
            load_adj(0, 1)

            def step(p, c):
                if there(c + 3):
                    wait(sp, xT_made, p + c + 2)
                    wait(sp, x_bo_set, p + c + 2)
                    load(p, c + 3)
                    wait(sp, kind_set, p + c + 2)
                    load_adj(p, c + 3)
                if there(c - 3):
                    wait(sp, out_set, p + c - 2)
                    sp.dma_start(out[p + c - 3].rearrange("(t p) d -> p t d", p=P),
                                 y1[:, (c - 3) % 2, :, :]).then_inc(stored[(c - 3) % 2], 16)

            steps(sp, step)
            for s in stored:
                sp.wait_ge(s, 16 * (G // 2))

        @block.tensor
        def _(pe):
            def product(dst, terms, lo_set, count):
                for n, ((a_hi, _), (b_hi, b_lo)) in enumerate(terms):
                    pe.matmul(dst, a_hi, b_lo, start=(n == 0), stop=False)
                    pe.matmul(dst, a_hi, b_hi, start=False, stop=False)
                wait(pe, lo_set, count)
                for n, ((_, a_lo), (b_hi, _)) in enumerate(terms):
                    mm = pe.matmul(dst, a_lo, b_hi, start=False, stop=(n == len(terms) - 1))
                return mm

            pe.wait_ge(ident_set, 1)
            for n, (w, ps) in enumerate(((wq_s, BS), (wk_s, BN0), (wv_s, BN1))):
                pe.wait_ge(qk_in if n < 2 else vo_in, 32)
                for k in range(C):
                    for e in range(C):
                        mm = pe.transpose(ps[:, e * D + k * P:e * D + (k + 1) * P],
                                          w[:, k, e * P:(e + 1) * P], ident[:, :])
                mm.then_inc(wT_made, 1)

            def weight_products():
                for n, (lhs, rhs, ps) in enumerate(((wqT, wkT, BZ0), (wvT, wo_s, BZ1))):
                    pe.wait_ge(wT_out, 2 + n)
                    for k in range(C):
                        for e in range(C):
                            mm = pe.matmul(ps[:, k * D:(k + 1) * D], lhs[:, e, k * P:(k + 1) * P],
                                           rhs[:, e, :], start=(e == 0), stop=(e == C - 1))
                    mm.then_inc(w_made, 1)

            def z_tile(p, c, t):
                for j in range(J):
                    cols = slice(j * N + t * P, j * N + (t + 1) * P)
                    mm = product(z_ps[t][:, j * D:(j + 1) * D],
                                 [((nb_hi[:, d, cols], nb_lo[:, d, cols]),
                                   (w1_hi[:, j * C + d, :], w1_lo[:, j * C + d, :])) for d in range(C)],
                                 nb_lo_set, C * (p + c - 1))
                mm.then_inc(z_made, 1)

            def nb_chunk(p, c, d):
                wait(pe, nb_lo_set, C * (p + c - 1) + d + 1)
                for n, part in enumerate((h_hi, h_lo)):
                    if d == 0:
                        wait(pe, (h_hi_set, h_lo_set)[n], p + c + 1)
                    for m in range(T):
                        mm = pe.matmul(nb_ps[d][:, :], part[:, m, d * P:(d + 1) * P],
                                       maskT[:, c % 2, m, :, :].rearrange("p j n -> p (j n)"),
                                       start=(n == 0 and m == 0), stop=(n == 1 and m == T - 1))
                mm.then_inc(nb_made, 1)

            def step(p, c):
                if there(c):
                    if c == 0:
                        pe.wait_ge(w_ready, 1)
                    wait(pe, xT_lo_set, p + c + 1)
                    for d in range(C):
                        cols = slice(d * P, (d + 1) * P)
                        mm = product(q_ps[:, d * N:(d + 1) * N],
                                     [((wqk_hi[:, k, cols], wqk_lo[:, k, cols]),
                                       (xT_hi[:, k, :], xT_lo[:, k, :])) for k in range(C)], w_ready, 1)
                    mm.then_inc(q_made, 1)
                if there(c - 2):
                    nb_chunk(p, c - 2, 1)
                if there(c):
                    if c == 0:
                        pe.wait_ge(w_ready, 2)
                    for t in range(T):
                        rows = slice(t * P, (t + 1) * P)
                        mm = product(v_ps[:, t * D:(t + 1) * D],
                                     [((xT_hi[:, k, rows], xT_lo[:, k, rows]),
                                       (wvo_hi[:, k, :], wvo_lo[:, k, :])) for k in range(C)],
                                     xT_lo_set, p + c + 1)
                    mm.then_inc(v_made, 1)
                    wait(pe, q_hi_set, p + c + 1)
                    wait(pe, degree_set, p + c - 1)
                    for t in range(T):
                        rows = slice(t * P, (t + 1) * P)
                        mm = product(s_ps[:, t * N:(t + 1) * N],
                                     [((qT_hi[:, d, rows], qT_lo[:, d, rows]),
                                       (xT_hi[:, d, :], xT_lo[:, d, :])) for d in range(C)],
                                     q_lo_set, p + c + 1)
                    mm.then_inc(s_made, 1)
                if there(c - 2):
                    if c == 2:
                        pe.wait_ge(w_ready, 3)
                    wait(pe, nb_hi_set, C * (p + c - 1))
                    wait(pe, y0_set, T * min(c, G) if isinstance(p, int) else T * (p + c))
                    wait(pe, z_b_set, T * (p + c - 3) + 1)
                    z_tile(p, c, 0)
                if there(c - 1):
                    wait(pe, masks_set, p + c)
                    wait(pe, scored, T * min(c + 1, G) if isinstance(p, int) else T * (p + c + 1))
                    for t in range(T):
                        for j in range(J):
                            for m in range(T):
                                mask_b = maskT[:, (c - 1) % 2, m, j, :].bitcast(BF16)[
                                    :, 2 * t * P + 1:2 * (t + 1) * P:2]
                                mm = pe.matmul(deg_ps[:, t * J + j:t * J + j + 1], mask_b, ones_b[:, :],
                                               start=(m == 0), stop=(m == T - 1))
                    mm.then_inc(deg_made, 1)
                if there(c + 1):
                    wait(pe, x_in[(c + 1) % 2], dma_count(p, c + 1))
                    wait(pe, v_lo_set, p + c + 1)
                    for t in range(T):
                        for k in range(C):
                            mm = pe.transpose(xT_ps[:, k * N + t * P:k * N + (t + 1) * P],
                                              x_s[:, (c + 1) % 2, t, k * P:(k + 1) * P], ident[:, :])
                    mm.then_inc(xT_made, 1)
                if there(c):
                    wait(pe, prob_set, T * (p + c + 1))
                    for t in range(T):
                        for m in range(T):
                            mm = pe.transpose(pT_ps[:, m * N + t * P:m * N + (t + 1) * P],
                                              prob[:, t, m * P:(m + 1) * P], ident[:, :])
                    mm.then_inc(pT_made, 1)
                if there(c - 2):
                    wait(pe, z_b_set, T * (p + c - 2))
                    z_tile(p, c, 1)
                if there(c):
                    wait(pe, pT_hi_set, p + c + 1)
                    wait(pe, v_lo_set, p + c + 1)
                    wait(pe, masks_set, p + c + 1)
                    for t in range(T):
                        if t == 1:
                            wait(pe, z_b_set, T * (p + c - 2) + 1)
                            wait(pe, y0_set, T * (p + c))
                        rows = slice(t * P, (t + 1) * P)
                        mm = product(o_ps[t][:, 0:D],
                                     [((pT_hi[:, m, rows], pT_lo[:, m, rows]),
                                       (v_hi[:, m, :], v_lo[:, m, :])) for m in range(T)],
                                     pT_lo_set, p + c + 1)
                        mm.then_inc(o_made, 1)
                if there(c - 1):
                    nb_chunk(p, c - 1, 0)
                if there(c + 1):
                    wait(pe, kind_set, p + c + 2)
                    if c == -1:
                        pe.wait_ge(ident_set, 2)
                    wait(pe, y0_set, T * (p + c) + 1)
                    for t in range(T):
                        for m in range(T):
                            mm = pe.transpose(kindT_ps[:, m * N + t * P:m * N + (t + 1) * P],
                                              kind[:, t, m * P:(m + 1) * P], ident_b[:, :])
                    mm.then_inc(kindT_made, 1)

            steps(pe, step, weight_products)

        @block.scalar
        def _(act):
            for w, s in ((Wv, wv_s), (Wo, wo_s)):
                act.dma_start(s[:, :, :], w.rearrange("(c p) e -> p c e", p=P)).then_inc(vo_in, 16)
            act.dma_start(w1_s[:, :, :], W1.rearrange("(c p) e -> p c e", p=P)).then_inc(w1_in, 16)
            for v, s in ((bo, bo_r), (gamma0, gamma0_r), (beta0, beta0_r), (gamma1, gamma1_r), (beta1, beta1_r)):
                for t in range(T):
                    act.dma_start(s[:, t, :], v.partition_broadcast(P)).then_inc(vectors_in, 16)
            act.dma_start(b1_r[:, :], b1.partition_broadcast(P)).then_inc(vectors_in, 16)

            def flat(a):
                return a[:, :, :].rearrange("p c n -> p (c n)")

            def norm(layer, p, g, t):
                y = y0[:, t, :] if layer == 0 else y1[:, g % 2, t, :]
                col = T * layer + t
                wait(act, shift_set[layer], p + g + 1)
                act.activation(y, y, ACT.Identity, bias=shift[:, g % 2, col:col + 1],
                               scale=rstd[:, g % 2, col:col + 1]).then_inc(norm_set[layer], 1)

            def squares(layer, p, g):
                y = y0[:, :, :] if layer == 0 else y1[:, g % 2, :, :]
                wait(act, mean_set[layer], p + g + 1)
                for t in range(T):
                    col = T * layer + t
                    act.activation(square[:, col, :], y[:, t, :], ACT.Square, scale=ROOT,
                                   bias=scaled_mean[:, g % 2, col:col + 1],
                                   accum_out=var[:, g % 2, col:col + 1]).then_inc(squares_set[layer], 1)

            def step(p, c):
                if there(c - 1):
                    squares(0, p, c - 1)
                if there(c - 2):
                    wait(act, nb_made, C * (p + c - 2) + 1)
                    act.activation(nb_hi[:, 0, :], nb_ps[0][:, :], ACT.Copy).then_inc(nb_hi_set, 1)
                if there(c):
                    wait(act, q_made, p + c + 1)
                    act.activation(flat(qT_hi), q_ps[:, :], ACT.Copy).then_inc(q_hi_set, 1)
                if there(c - 2):
                    wait(act, nb_made, C * (p + c - 1))
                    act.activation(nb_hi[:, 1, :], nb_ps[1][:, :], ACT.Copy).then_inc(nb_hi_set, 1)
                if there(c - 1):
                    norm(0, p, c - 1, 0)
                if there(c):
                    wait(act, v_made, p + c + 1)
                    act.activation(flat(v_hi), v_ps[:, :], ACT.Copy).then_inc(v_hi_set, 1)
                if there(c - 1):
                    norm(0, p, c - 1, 1)
                if there(c - 3):
                    squares(1, p, c - 3)
                if there(c):
                    for t in range(T):
                        wait(act, scored, T * (p + c) + t + 1)
                        act.activation(prob[:, t, :], neg_score[:, t, :], ACT.Exp, scale=-1.0,
                                       bias=neg_max[:, t:t + 1],
                                       accum_out=prob_sum[:, c % 2, t:t + 1]).then_inc(prob_set, 1)
                    wait(act, pT_made, p + c + 1)
                    act.activation(flat(pT_hi), pT_ps[:, :], ACT.Copy).then_inc(pT_hi_set, 1)
                if there(c - 1):
                    wait(act, h_set, p + c)
                    wait(act, nb_made, C * (p + c - 1))
                    act.activation(flat(h_hi), h[:, (c - 1) % 2, :, :].rearrange("p t d -> p (t d)"),
                                   ACT.Copy).then_inc(h_hi_set, 1)
                if there(c + 1):
                    wait(act, xT_made, p + c + 2)
                    act.activation(flat(xT_hi), xT_ps[:, :], ACT.Copy).then_inc(xT_hi_set, 1)
                if there(c - 3):
                    for t in range(T):
                        norm(1, p, c - 3, t)

            def weight_hi_parts():
                for n, (hi, ps) in enumerate(((wqk_hi, BZ0), (wvo_hi, BZ1))):
                    act.wait_ge(w_made, n + 1)
                    act.activation(flat(hi), ps[:, :], ACT.Copy).then_inc(w_hi_set, 1)
                act.wait_ge(w1_in, 16)
                act.activation(flat(w1_hi), flat(w1_s), ACT.Copy).then_inc(w_hi_set, 1)

            steps(act, step, weight_hi_parts)

        @block.vector
        def _(dve):
            def flat(a):
                return a[:, :, :].rearrange("p c n -> p (c n)")

            def low(lo, full, hi):
                return dve.tensor_tensor(lo, full, hi.bitcast(F32), ALU.subtract)

            for n, (wT, ps) in enumerate(((wqT, BS), (wkT, BN0), (wvT, BN1))):
                dve.wait_ge(wT_made, n + 1)
                dve.tensor_copy(flat(wT), ps[:, :]).then_inc(wT_out, 1)

            def weight_lo_parts():
                for n, (lo, full, hi) in enumerate(((wqk_lo, BZ0[:, :], wqk_hi), (wvo_lo, BZ1[:, :], wvo_hi),
                                                    (w1_lo, flat(w1_s), w1_hi))):
                    dve.wait_ge(w_hi_set, n + 1)
                    low(flat(lo), full, flat(hi)).then_inc(w_ready, 1)

            def mask(p, c, j):
                ins = dve.tensor_scalar(maskT[:, c % 2, :, j, :],
                                        kindT_ps.rearrange("p (m n) -> p m n", m=T),
                                        float(j + 1), None, ALU.is_equal)
                if j == J - 1:
                    ins.then_inc(masks_set, 1)

            def edge_kind(p, c):
                wait(dve, adj_in[c % 2], dma_count(p, c))
                wait(dve, kindT_made, p + c)
                wait(dve, no_edge_set, p + c)
                dve.tensor_scalar(kind[:, :, :], adj_s[:, c % 2, :, :], -1.0, 3.0, ALU.max, ALU.min)\
                   .then_inc(kind_set, 1)

            def edge_mask(p, c):
                wait(dve, kind_set, p + c + 1)
                dve.tensor_scalar(no_edge[:, c % 2, :, :], kind[:, :, :], 0.0, MASKED,
                                  ALU.is_equal, ALU.mult).then_inc(no_edge_set, 1)

            def z_first(p, c, t):
                wait(dve, z_made, T * (p + c) + t + 1)
                wait(dve, inv_degree_set, p + c + 1)
                dve.scalar_tensor_tensor(out=z_a[:, t, :], in0=z_ps[t][:, 0:D],
                                         scalar=inv_degree[:, c % 2, t * J:t * J + 1], in1=b1_r[:, :],
                                         op0=ALU.mult, op1=ALU.add).then_inc(z_a_set, 1)

            def z_second(p, c, t):
                wait(dve, z_a_set, T * (p + c) + t + 1)
                dve.scalar_tensor_tensor(out=z_b[:, t, :], in0=z_ps[t][:, D:2 * D],
                                         scalar=inv_degree[:, c % 2, t * J + 1:t * J + 2],
                                         in1=z_a[:, t, :], op0=ALU.mult, op1=ALU.add).then_inc(z_b_set, 1)

            def relu_residual(p, c, t):
                wait(dve, z_b_set, T * (p + c) + t + 1)
                wait(dve, stored[c % 2], dma_count(p, c - 2))
                dve.scalar_tensor_tensor(out=y1[:, c % 2, t, :], in0=z_b[:, t, :], scalar=0.0,
                                         in1=h[:, c % 2, t, :], op0=ALU.max, op1=ALU.add,
                                         accum_out=ln_sum[:, c % 2, T + t:T + t + 1]).then_inc(y1_set, 1)

            def attention_residual(p, c, t):
                wait(dve, o_made, T * (p + c) + t + 1)
                wait(dve, inv_sum_set, p + c + 1)
                wait(dve, x_bo_set, p + c + 1)
                wait(dve, h_set, p + c)
                dve.scalar_tensor_tensor(out=y0[:, t, :], in0=o_ps[t][:, 0:D], scalar=inv_sum[:, t:t + 1],
                                         in1=x_bo[:, c % 2, t, :], op0=ALU.mult, op1=ALU.add,
                                         accum_out=ln_sum[:, c % 2, t:t + 1]).then_inc(y0_set, 1)

            def means(layer, p, g):
                s = slice(T * layer, T * (layer + 1))
                wait(dve, (y0_set, y1_set)[layer], T * (p + g + 1))
                wait(dve, shift_set[layer], p + g - 1)
                dve.tensor_scalar(scaled_mean[:, g % 2, s], ln_sum[:, g % 2, s], -ROOT / D, None, ALU.mult)\
                   .then_inc(mean_set[layer], 1)
                dve.tensor_scalar(neg_mean[:, g % 2, s], ln_sum[:, g % 2, s], -1.0 / D, None, ALU.mult)\
                   .then_inc(neg_mean_set[layer], 1)

            def step(p, c):
                if there(c + 1):
                    edge_kind(p, c + 1)
                if there(c - 2):
                    wait(dve, nb_hi_set, C * (p + c - 2) + 1)
                    low(nb_lo[:, 0, :], nb_ps[0][:, :], nb_hi[:, 0, :]).then_inc(nb_lo_set, 1)
                if there(c):
                    wait(dve, q_hi_set, p + c + 1)
                    low(flat(qT_lo), q_ps[:, :], flat(qT_hi)).then_inc(q_lo_set, 1)
                if there(c - 2):
                    wait(dve, nb_hi_set, C * (p + c - 1))
                    low(nb_lo[:, 1, :], nb_ps[1][:, :], nb_hi[:, 1, :]).then_inc(nb_lo_set, 1)
                if there(c):
                    wait(dve, kindT_made, p + c + 1)
                    wait(dve, nb_made, C * (p + c - 1))
                    wait(dve, deg_made, p + c - 1)
                    mask(p, c, 0)
                    wait(dve, v_hi_set, p + c + 1)
                    low(flat(v_lo), v_ps[:, :], flat(v_hi)).then_inc(v_lo_set, 1)
                    dve.wait_ge(vectors_in, VECTORS_IN)
                    wait(dve, s_made, p + c + 1)
                    wait(dve, no_edge_set, p + c + 1)
                    for t in range(T):
                        dve.tensor_tensor_reduce(out=neg_score[:, t, :], in0=s_ps[:, t * N:(t + 1) * N],
                                                 in1=no_edge[:, c % 2, t, :], scale=-SCALE, scalar=3.0e38,
                                                 op0=ALU.add, op1=ALU.min,
                                                 accum_out=neg_max[:, t:t + 1]).then_inc(scored, 1)
                    mask(p, c, 1)
                if there(c - 2):
                    z_first(p, c - 2, 0)
                if there(c - 1):
                    wait(dve, deg_made, p + c)
                    dve.tensor_scalar(degree[:, :], deg_ps, DEGREE_EPS, None, ALU.add).then_inc(degree_set, 1)
                if there(c + 1):
                    edge_mask(p, c + 1)
                if there(c - 2):
                    z_second(p, c - 2, 0)
                if there(c - 1):
                    wait(dve, degree_set, p + c)
                    dve.reciprocal(inv_degree[:, (c - 1) % 2, :], degree[:, :]).then_inc(inv_degree_set, 1)
                if there(c - 2):
                    relu_residual(p, c - 2, 0)
                if there(c):
                    wait(dve, pT_hi_set, p + c + 1)
                    low(flat(pT_lo), pT_ps[:, :], flat(pT_hi)).then_inc(pT_lo_set, 1)
                    wait(dve, prob_set, T * (p + c + 1))
                    dve.reciprocal(inv_sum[:, :], prob_sum[:, c % 2, :]).then_inc(inv_sum_set, 1)
                if there(c + 1):
                    wait(dve, xT_hi_set, p + c + 2)
                    low(flat(xT_lo), xT_ps[:, :], flat(xT_hi)).then_inc(xT_lo_set, 1)
                if there(c - 2):
                    z_first(p, c - 2, 1)
                if there(c):
                    attention_residual(p, c, 0)
                if there(c - 2):
                    z_second(p, c - 2, 1)
                if there(c):
                    attention_residual(p, c, 1)
                if there(c - 2):
                    relu_residual(p, c - 2, 1)
                if there(c):
                    means(0, p, c)
                if there(c - 2):
                    means(1, p, c - 2)

            steps(dve, step, weight_lo_parts)

        @block.gpsimd
        def _(pool):
            for n, m in enumerate((ident, ident_b)):
                pool.memset(m[:, :], 0.0).then_inc(zeros_set, 1)
                pool.wait_ge(zeros_set, n + 1)
                pool.affine_select(out=m[:, :], in_=m[:, :], compare_op=ALU.not_equal, fill=1.0, base=0,
                                   pattern=[[-1, P]], channel_multiplier=1).then_inc(ident_set, 1)
            pool.memset(ones_b[:, :], 1.0).then_inc(const_set, 1)
            for m, value in ((minus_half, -0.5), (eps_c, LN_EPS)):
                pool.memset(m[:, :], value).then_inc(const_set, 1)
            pool.wait_ge(const_set, 3)
            pool.wait_ge(vectors_in, VECTORS_IN)

            def statistics(layer, p, g):
                s = slice(T * layer, T * (layer + 1))
                wait(pool, squares_set[layer], T * (p + g + 1))
                pool.tensor_tensor(var_eps[:, s], var[:, g % 2, s], eps_c[:, s], ALU.add)\
                    .then_inc(var_set[layer], 1)
                wait(pool, var_set[layer], p + g + 1)
                pool.tensor_tensor(rstd[:, g % 2, s], var_eps[:, s], minus_half[:, s], ALU.pow)\
                    .then_inc(rstd_set[layer], 1)
                wait(pool, rstd_set[layer], p + g + 1)
                wait(pool, neg_mean_set[layer], p + g + 1)
                pool.tensor_tensor(shift[:, g % 2, s], neg_mean[:, g % 2, s], rstd[:, g % 2, s], ALU.mult)\
                    .then_inc(shift_set[layer], 1)

            def step(p, c):
                if there(c - 1):
                    statistics(0, p, c - 1)
                if there(c + 1):
                    g = (c + 1) % 2
                    wait(pool, x_in[g], dma_count(p, c + 1))
                    wait(pool, y0_set, T * (p + c))
                    pool.tensor_tensor(x_bo[:, g, :, :], x_s[:, g, :, :], bo_r[:, :, :], ALU.add)\
                        .then_inc(x_bo_set, 1)
                if there(c - 1):
                    g = (c - 1) % 2
                    wait(pool, norm_set[0], T * (p + c))
                    pool.tensor_tensor(y0[:, :, :], y0[:, :, :], gamma0_r[:, :, :], ALU.mult)\
                        .then_inc(scaled0, 1)
                    wait(pool, scaled0, p + c)
                    wait(pool, y1_set, T * (p + c - 2))
                    pool.tensor_tensor(h[:, g, :, :], y0[:, :, :], beta0_r[:, :, :], ALU.add)\
                        .then_inc(h_set, 1)
                if there(c - 3):
                    statistics(1, p, c - 3)
                if there(c - 1):
                    wait(pool, h_hi_set, p + c)
                    wait(pool, nb_made, C * (p + c - 1))
                    pool.tensor_tensor(h_lo[:, :, :], h[:, g, :, :], h_hi[:, :, :].bitcast(F32),
                                       ALU.subtract).then_inc(h_lo_set, 1)
                if there(c - 3):
                    y = y1[:, (c - 3) % 2, :, :]
                    wait(pool, norm_set[1], T * (p + c - 2))
                    pool.tensor_tensor(y, y, gamma1_r[:, :, :], ALU.mult).then_inc(scaled1, 1)
                    wait(pool, scaled1, p + c - 2)
                    pool.tensor_tensor(y, y, beta1_r[:, :, :], ALU.add).then_inc(out_set, 1)

            steps(pool, step)


_INS = ['x', 'adj', 'L0_gnn_Wq', 'L0_gnn_Wk', 'L0_gnn_Wv', 'L0_gnn_Wo', 'L0_gnn_bo', 'L0_gnn_gamma',
        'L0_gnn_beta', 'L1_gnn_W', 'L1_gnn_b', 'L1_gnn_gamma', 'L1_gnn_beta']


def kernel(**inputs):
    import numpy as _np
    import concourse.bacc as _bacc
    from concourse import mybir as _mybir
    from concourse.bass_utils import run_bass_kernel_spmd as _run

    nc = _bacc.Bacc("TRN2", target_bir_lowering=False, num_devices=1)
    arrays, args = {}, []
    for name in _INS:
        a = _np.ascontiguousarray(inputs[name])
        arrays[f"in_{name}_dram"] = a
        args.append(nc.dram_tensor(f"in_{name}_dram", a.shape, _mybir.dt.from_np(a.dtype),
                                   kind="ExternalInput").ap())
    args.append(nc.dram_tensor("out_dram", inputs["x"].shape, _mybir.dt.float32, kind="ExternalOutput").ap())
    gnn_kernel(nc, *args)
    r = _run(nc, [arrays], core_ids=[0])
    return r.results[0]["out_dram"]
```
